# Optimizing a Trainium2 kernel written in Bass

```python
import numpy as np
import jax
import jax.numpy as jnp

def _softmax(x, axis=-1):
    return jax.nn.softmax(x, axis=axis)

def _gelu(x):
    return jax.nn.gelu(x, approximate=True)

def _silu(x):
    return jax.nn.silu(x)

def _sigmoid(x):
    return jax.nn.sigmoid(x)

def _layernorm(x, axis=-1, eps=1e-05):
    m = jnp.mean(x, axis=axis, keepdims=True)
    v = jnp.var(x, axis=axis, keepdims=True)
    return (x - m) / jnp.sqrt(v + eps)

def _scatter_add(tgt, idx, src, axis=0):
    return tgt.at[idx].add(src)

def _segment_sum(src, seg, n):
    return jax.ops.segment_sum(src, seg, n)
kernel_name = 'mk_rec_standalone_d1_rec_r8_c98735'

def setup_inputs(seed: int=0):
    np.random.seed(seed)
    _w = jnp.asarray

    def _rec_inputs():
        import jax
        import jax.numpy as jnp
        _rk = jax.random.key(seed)
        r_white_features = jax.random.uniform(jax.random.fold_in(_rk, 1), (512, 5120), jnp.float32, 0.0, 1)
        r_black_features = jax.random.uniform(jax.random.fold_in(_rk, 2), (512, 5120), jnp.float32, 0.0, 1)
        return (r_white_features, r_black_features)
    r_white_features, r_black_features = _rec_inputs()

    def _L0_rec_setup():
        import jax, jax.numpy as jnp
        import numpy as np
        FEATURE_SIZE = 5120
        FIRST_HIDDEN = 512
        HALF = FIRST_HIDDEN // 2
        SECOND_HIDDEN = 32
        BATCH = 512

        def _clipped_relu(x):
            return jnp.clip(x, 0.0, 1.0)
        key = jax.random.key(seed)
        ks = jax.random.split(key, 10)
        inp = {'white_features': jax.random.uniform(ks[0], (BATCH, FEATURE_SIZE), dtype=jnp.float32), 'black_features': jax.random.uniform(ks[1], (BATCH, FEATURE_SIZE), dtype=jnp.float32), 'w_in': jax.random.normal(ks[2], (HALF, FEATURE_SIZE), dtype=jnp.float32) * 0.1, 'b_in': jnp.zeros((HALF,), dtype=jnp.float32), 'w_h1': jax.random.normal(ks[3], (SECOND_HIDDEN, FIRST_HIDDEN), dtype=jnp.float32) * 0.1, 'b_h1': jnp.zeros((SECOND_HIDDEN,), dtype=jnp.float32), 'w_h2': jax.random.normal(ks[4], (SECOND_HIDDEN, SECOND_HIDDEN), dtype=jnp.float32) * 0.1, 'b_h2': jnp.zeros((SECOND_HIDDEN,), dtype=jnp.float32), 'w_out': jax.random.normal(ks[5], (1, SECOND_HIDDEN), dtype=jnp.float32) * 0.1, 'b_out': jnp.zeros((1,), dtype=jnp.float32)}
        return inp
    _L0_rec_all = _L0_rec_setup()
    _L0_rec_in = {k: v for k, v in _L0_rec_all.items() if k in ('w_in', 'b_in', 'w_h1', 'b_h1', 'w_h2', 'b_h2', 'w_out', 'b_out')}
    del _L0_rec_all
    return {'r_white_features': r_white_features, 'r_black_features': r_black_features, 'L0_rec_w_in': _L0_rec_in['w_in'], 'L0_rec_b_in': _L0_rec_in['b_in'], 'L0_rec_w_h1': _L0_rec_in['w_h1'], 'L0_rec_b_h1': _L0_rec_in['b_h1'], 'L0_rec_w_h2': _L0_rec_in['w_h2'], 'L0_rec_b_h2': _L0_rec_in['b_h2'], 'L0_rec_w_out': _L0_rec_in['w_out'], 'L0_rec_b_out': _L0_rec_in['b_out']}

def reference(r_white_features, r_black_features, L0_rec_w_in, L0_rec_b_in, L0_rec_w_h1, L0_rec_b_h1, L0_rec_w_h2, L0_rec_b_h2, L0_rec_w_out, L0_rec_b_out):
    import jax
    import jax.numpy as jnp

    def _L0_rec_ref(white_features, black_features, w_in, b_in, w_h1, b_h1, w_h2, b_h2, w_out, b_out):
        import jax, jax.numpy as jnp
        import numpy as np
        FEATURE_SIZE = 5120
        FIRST_HIDDEN = 512
        HALF = FIRST_HIDDEN // 2
        SECOND_HIDDEN = 32
        BATCH = 512

        def _clipped_relu(x):
            return jnp.clip(x, 0.0, 1.0)
        out1 = white_features @ w_in.T + b_in
        out2 = black_features @ w_in.T + b_in
        x = _clipped_relu(jnp.concatenate([out1, out2], axis=1))
        x = _clipped_relu(x @ w_h1.T + b_h1)
        x = _clipped_relu(x @ w_h2.T + b_h2)
        return x @ w_out.T + b_out
    y = _L0_rec_ref(r_white_features, r_black_features, L0_rec_w_in, L0_rec_b_in, L0_rec_w_h1, L0_rec_b_h1, L0_rec_w_h2, L0_rec_b_h2, L0_rec_w_out, L0_rec_b_out)
    return y

_drawn_inputs = setup_inputs


def setup_inputs(seed=0):
    import zlib

    import numpy as np

    out = dict(_drawn_inputs(seed))
    spreads = {'L0_rec_b_in': (0.0, 0.1), 'L0_rec_b_h1': (0.0, 0.1), 'L0_rec_b_h2': (0.0, 0.1)}
    factors = {}
    for name, (base, spread) in spreads.items():
        noise = np.random.default_rng([zlib.crc32(name.encode()), seed]).standard_normal(out[name].shape)
        drawn = base * np.exp(spread * noise) if base else spread * noise
        out[name] = jnp.asarray(drawn.astype(out[name].dtype))
    for name, factor in factors.items():
        out[name] = (out[name] * factor).astype(out[name].dtype)
    return out
```

```python
from contextlib import ExitStack

import concourse.bass as bass
from concourse import mybir

F32 = mybir.dt.float32
F32R = mybir.dt.float32r
BF16 = mybir.dt.bfloat16
ALU = mybir.AluOpType
ACT = mybir.ActivationFunctionType

P = 128
TILES_PER_CHUNK = 2
SLOTS = 4
WARM_UP_MATMULS = 8


def build(nc, features, params, bias_rows, out):
    n_features, width = features.shape
    batch = out.shape[0]
    hidden = width - 2 * batch
    halves = hidden // P
    quarters = 4
    quarter = batch // quarters
    units = P // quarters
    assert quarter == P and batch == 512 and halves == 2

    TC = TILES_PER_CHUNK
    chunks = n_features // (P * TC)
    first_looped = 2
    last_chunks = 2
    looped = chunks - first_looped - last_chunks
    assert n_features == chunks * P * TC and looped % SLOTS == 0
    turns = looped // SLOTS

    W = slice(0, hidden)
    WHITE = slice(hidden, hidden + batch)
    BLACK = slice(hidden + batch, width)
    SIDES = (WHITE, BLACK)

    n_h1 = 2 * halves * units
    H2_AT, OUT_AT, B_IN_AT = n_h1, n_h1 + P, n_h1 + P + quarters
    n_params = B_IN_AT + halves
    assert params.shape[1] == n_params

    chunk_dram = features.rearrange("(c p t) n -> c p t n", p=P, t=TC)
    out_dram = out.rearrange("(j n) o -> j (n o)", j=quarters)

    with ExitStack() as ctx:
        def sb(name, shape, dt):
            return ctx.enter_context(nc.sbuf_tensor(name, shape, dt))

        def psum(name, shape):
            return ctx.enter_context(nc.psum_tensor(name, shape, F32))

        def sem(name):
            return ctx.enter_context(nc.semaphore(name))

        raw = [sb(f"raw{s}", [P, TC, width], F32) for s in range(SLOTS)]
        hi = [sb(f"hi{s}", [P, TC, width], F32R) for s in range(SLOTS)]
        lo = [sb(f"lo{s}", [P, TC, width], F32R) for s in range(SLOTS)]
        par = sb("par", [P, n_params], F32)
        rows = sb("rows", [1, bias_rows.shape[1]], F32)
        ones = sb("ones", [1, P], F32)
        zeros = sb("zeros", [P, batch], BF16)
        x_relu = sb("x_relu", [P, 4, batch], F32)
        x_act = sb("x_act", [P, 4, batch], F32)
        h1_act = sb("h1_act", [P, P], F32)
        h2_act = sb("h2_act", [P, P], F32)
        y = sb("y", [quarters, P], F32)

        x_acc = [psum(f"x_acc{b}", [P, batch]) for b in range(4)]
        h1_acc = psum("h1_acc", [P, 512])
        h2_acc = psum("h2_acc", [P, 512])
        y_acc = psum("y_acc", [P, 512])
        warm = psum("warm", [P, 512])

        slot_loaded = [sem(f"slot_loaded{s}") for s in range(SLOTS)]
        first_loaded = [sem(f"first_loaded{i}") for i in range(3)]
        params_loaded = sem("params_loaded")
        rows_loaded = sem("rows_loaded")
        constants_set = sem("constants_set")
        first_hi = sem("first_hi")
        first_w_hi = sem("first_w_hi")
        first_lo = sem("first_lo")
        hi_ready = sem("hi_ready")
        lo_ready = sem("lo_ready")
        chunks_used = sem("chunks_used")
        x_summed = sem("x_summed")
        x_relu_ready = sem("x_relu_ready")
        x_ready = sem("x_ready")
        h1_summed = sem("h1_summed")
        h1_ready = sem("h1_ready")
        h2_summed = sem("h2_summed")
        h2_ready = sem("h2_ready")
        y_summed = sem("y_summed")
        y_ready = sem("y_ready")
        y_stored = sem("y_stored")

        block = ctx.enter_context(nc.Block())

        @block.sync
        def _(sp):
            sp.dma_start(raw[0][:, 0, 0:BLACK.start], chunk_dram[0, :, 0, 0:BLACK.start]).then_inc(first_loaded[0], 16)
            sp.dma_start(raw[0][:, 0, BLACK], chunk_dram[0, :, 0, BLACK]).then_inc(first_loaded[1], 16)
            sp.dma_start(raw[0][:, 1, :], chunk_dram[0, :, 1, :]).then_inc(first_loaded[2], 16)
            for s in range(1, SLOTS):
                sp.dma_start(raw[s][:, :, :], chunk_dram[s]).then_inc(slot_loaded[s], 16)
            with sp.Fori(0, turns) as turn:
                for i in range(SLOTS):
                    c = turn * SLOTS + (SLOTS + i)
                    if i == 0:
                        sp.wait_ge(lo_ready, turn * SLOTS + 1)
                    else:
                        sp.wait_ge(lo_ready, turn * SLOTS + (i + 1))
                    sp.dma_start(raw[i][:, :, :], chunk_dram[c]).then_inc(slot_loaded[i], 16)
            sp.wait_ge(y_ready, 1)
            sp.dma_start(out_dram, y[:, :]).then_inc(y_stored, 16)
            sp.wait_ge(y_stored, 16)

        @block.gpsimd
        def _(pool):
            pool.memset(zeros[:, :], 0.0).then_inc(constants_set, 1)
            pool.memset(ones[:, :], 1.0).then_inc(constants_set, 1)

        @block.scalar
        def _(act):
            act.dma_start(rows[:, :], bias_rows).then_inc(rows_loaded, 16)
            act.dma_start(par[:, :], params).then_inc(params_loaded, 16)

            act.wait_ge(first_loaded[0], 16)
            act.activation(hi[0][:, 0, WHITE], raw[0][:, 0, WHITE], ACT.Copy).then_inc(first_hi, 1)
            act.wait_ge(first_loaded[1], 16)
            act.activation(hi[0][:, 0, BLACK], raw[0][:, 0, BLACK], ACT.Copy).then_inc(first_hi, 1)
            act.wait_ge(first_loaded[2], 16)
            act.activation(hi[0][:, 1, :], raw[0][:, 1, :], ACT.Copy).then_inc(hi_ready, 1)

            for s in range(1, SLOTS):
                act.wait_ge(slot_loaded[s], 16)
                act.activation(hi[s][:, :, :], raw[s][:, :, :], ACT.Copy).then_inc(hi_ready, 1)

            with act.Fori(0, turns) as turn:
                for i in range(SLOTS):
                    loads_before = 0 if i == 0 else 1
                    act.wait_ge(slot_loaded[i], turn * 16 + 16 * (loads_before + 1))
                    act.wait_ge(chunks_used, turn * SLOTS + (i + 1))
                    act.activation(hi[i][:, :, :], raw[i][:, :, :], ACT.Copy).then_inc(hi_ready, 1)

            act.wait_ge(params_loaded, 16)
            for b in range(4):
                act.wait_ge(x_summed, b + 1)
                for q in range(2):
                    cols = slice(q * batch // 2, (q + 1) * batch // 2)
                    act.activation(x_relu[:, b, cols], x_acc[b][:, cols], ACT.Relu,
                                   bias=par[:, B_IN_AT + b % 2:B_IN_AT + b % 2 + 1]).then_inc(x_relu_ready, 1)

        @block.vector
        def _(dve):
            def low_part(s, t, cols, signal):
                dve.tensor_tensor(lo[s][:, t, cols], raw[s][:, t, cols], hi[s][:, t, cols].bitcast(F32),
                                  ALU.subtract).then_inc(signal, 1)

            ALL = slice(0, width)
            TILES = slice(0, TC)
            dve.wait_ge(first_loaded[0], 16)
            dve.tensor_copy(hi[0][:, 0, W], raw[0][:, 0, W]).then_inc(first_w_hi, 1)
            dve.wait_ge(first_w_hi, 1)
            low_part(0, 0, W, first_lo)
            dve.wait_ge(first_hi, 1)
            low_part(0, 0, WHITE, first_lo)
            dve.wait_ge(first_hi, 2)
            low_part(0, 0, BLACK, first_lo)
            dve.wait_ge(hi_ready, 1)
            low_part(0, 1, ALL, lo_ready)

            for s in range(1, SLOTS):
                dve.wait_ge(hi_ready, s + 1)
                low_part(s, TILES, ALL, lo_ready)

            with dve.Fori(0, turns) as turn:
                for i in range(SLOTS):
                    dve.wait_ge(hi_ready, turn * SLOTS + (SLOTS + i + 1))
                    dve.wait_ge(chunks_used, turn * SLOTS + (i + 1))
                    low_part(i, TILES, ALL, lo_ready)

            for b in range(4):
                for q in range(2):
                    cols = slice(q * batch // 2, (q + 1) * batch // 2)
                    dve.wait_ge(x_relu_ready, 2 * b + q + 1)
                    dve.tensor_scalar(x_act[:, b, cols], x_relu[:, b, cols], 1.0, None, ALU.min).then_inc(x_ready, 1)
            dve.wait_ge(h1_summed, 1)
            dve.tensor_scalar(h1_act[:, :], h1_acc[:, 0:P], 0.0, 1.0, ALU.max, ALU.min).then_inc(h1_ready, 1)
            dve.wait_ge(h2_summed, 1)
            dve.tensor_scalar(h2_act[:, :], h2_acc[:, 0:P], 0.0, 1.0, ALU.max, ALU.min).then_inc(h2_ready, 1)
            dve.wait_ge(y_summed, 1)
            dve.tensor_copy(y[:, :], y_acc[0:quarters, 0:P]).then_inc(y_ready, 1)

        @block.tensor
        def _(pe):
            def product(b, w_part, x_part, s, t, start=False, stop=False):
                half = b % 2
                return pe.matmul(x_acc[b][:, :], w_part[s][:, t, half * P:(half + 1) * P],
                                 x_part[s][:, t, SIDES[b // 2]], start=start, stop=stop)

            def tile(s, t):
                for b in range(4):
                    product(b, hi, hi, s, t)
                for b in range(4):
                    product(b, hi, lo, s, t)
                for b in range(4):
                    last = product(b, lo, hi, s, t)
                return last

            pe.wait_ge(constants_set, 1)
            for _ in range(WARM_UP_MATMULS):
                pe.matmul(warm[:, :], zeros[:, 0:P], zeros[:, :], start=True, stop=True)

            pe.wait_ge(first_w_hi, 1)
            for side in range(2):
                pe.wait_ge(first_hi, side + 1)
                for half in range(halves):
                    product(2 * side + half, hi, hi, 0, 0, start=True)
            pe.wait_ge(first_lo, 1)
            for b in range(4):
                product(b, lo, hi, 0, 0)
            for side in range(2):
                pe.wait_ge(first_lo, side + 2)
                for half in range(halves):
                    product(2 * side + half, hi, lo, 0, 0)
            pe.wait_ge(hi_ready, 1)
            pe.wait_ge(lo_ready, 1)
            tile(0, 1).then_inc(chunks_used, 1)

            def chunk(s):
                for t in range(TC):
                    last = tile(s, t)
                return last

            pe.wait_ge(lo_ready, 2)
            chunk(1).then_inc(chunks_used, 1)
            with pe.Fori(0, turns) as turn:
                for i in range(SLOTS):
                    s = (first_looped + i) % SLOTS
                    pe.wait_ge(lo_ready, turn * SLOTS + (first_looped + i + 1))
                    chunk(s).then_inc(chunks_used, 1)

            def h1_products(b):
                for q in range(2):
                    pe.wait_ge(x_ready, 2 * b + q + 1)
                    for j in range(2 * q, 2 * q + 2):
                        last = pe.matmul(h1_acc[j * units:(j + 1) * units, 0:P], par[:, b * units:(b + 1) * units],
                                         x_act[:, b, j * quarter:(j + 1) * quarter],
                                         start=False, stop=(b == 3), skip_group_check=True)
                return last

            pe.wait_ge(lo_ready, chunks)
            for b in range(4):
                if b == 1:
                    pe.wait_ge(rows_loaded, 16)
                    pe.wait_ge(params_loaded, 16)
                    pe.wait_ge(constants_set, 2)
                    pe.matmul(h1_acc[:, 0:P], rows[:, 0:P], ones[:, :], start=True, stop=False, skip_group_check=True)
                    pe.matmul(h2_acc[:, 0:P], rows[:, P:2 * P], ones[:, :], start=True, stop=False)
                    pe.matmul(y_acc[0:quarters, 0:P], rows[:, 2 * P:2 * P + quarters], ones[:, :], start=True, stop=False)
                n = 0
                for c in range(chunks - last_chunks, chunks):
                    for t in range(TC):
                        for w_part, x_part in ((hi, hi), (hi, lo), (lo, hi)):
                            n += 1
                            last = product(b, w_part, x_part, c % SLOTS, t, stop=(n == 3 * TC * last_chunks))
                last.then_inc(x_summed, 1)
                if b >= 1:
                    h1_products(b - 1)
            h1_products(3).then_inc(h1_summed, 1)
            pe.wait_ge(h1_ready, 1)
            pe.matmul(h2_acc[:, 0:P], par[:, H2_AT:H2_AT + P], h1_act[:, :], start=False, stop=True).then_inc(h2_summed, 1)
            pe.wait_ge(h2_ready, 1)
            pe.matmul(y_acc[0:quarters, 0:P], par[:, OUT_AT:OUT_AT + quarters], h2_act[:, :],
                      start=False, stop=True).then_inc(y_summed, 1)


def kernel(r_white_features, r_black_features, L0_rec_w_in, L0_rec_b_in, L0_rec_w_h1, L0_rec_b_h1,
           L0_rec_w_h2, L0_rec_b_h2, L0_rec_w_out, L0_rec_b_out):
    import numpy as np
    import concourse.bacc as bacc
    from concourse.bass_utils import run_bass_kernel_spmd

    white, black, w_in = (np.asarray(a) for a in (r_white_features, r_black_features, L0_rec_w_in))
    w_h1, w_h2, w_out = (np.asarray(a) for a in (L0_rec_w_h1, L0_rec_w_h2, L0_rec_w_out))
    b_in, b_h1, b_h2, b_out = (np.asarray(a) for a in (L0_rec_b_in, L0_rec_b_h1, L0_rec_b_h2, L0_rec_b_out))
    batch = white.shape[0]
    units, joined = w_h1.shape
    quarters = P // units

    features = np.ascontiguousarray(np.concatenate([w_in.T, white.T, black.T], axis=1))

    h1_part = w_h1.T.reshape(joined // P, P, units).transpose(1, 0, 2).reshape(P, -1)
    h2_part = np.zeros((P, P), w_h2.dtype)
    out_part = np.zeros((P, quarters), w_out.dtype)
    for j in range(quarters):
        h2_part[j * units:(j + 1) * units, j * units:(j + 1) * units] = w_h2.T
        out_part[j * units:(j + 1) * units, j] = w_out[0]
    params = np.ascontiguousarray(np.concatenate([h1_part, h2_part, out_part, b_in.reshape(-1, P).T], axis=1))
    bias_rows = np.concatenate([np.tile(b_h1, quarters), np.tile(b_h2, quarters), np.tile(b_out, quarters)])[None]

    nc = bacc.Bacc("TRN2", target_bir_lowering=False, num_devices=1)
    arrays = {"features": features, "params": params, "bias_rows": bias_rows}
    ins = [nc.dram_tensor(n, a.shape, mybir.dt.from_np(a.dtype), kind="ExternalInput").ap() for n, a in arrays.items()]
    out = nc.dram_tensor("out", (batch, 1), F32, kind="ExternalOutput").ap()
    build(nc, *ins, out)
    result = run_bass_kernel_spmd(nc, [arrays], core_ids=[0])
    return result.results[0]["out"]
```

```python
from contextlib import ExitStack

import concourse.bass as bass
from concourse import mybir

F32 = mybir.dt.float32
F32R = mybir.dt.float32r
BF16 = mybir.dt.bfloat16
ALU = mybir.AluOpType
ACT = mybir.ActivationFunctionType

P = 128
TILES_PER_CHUNK = 2
SLOTS = 4
EARLY = 2
FIRST_LOOPED = 2
LAST_CHUNKS = 2
WARM_UP_MATMULS = 26


def build(nc, features, params, bias_rows, out):
    n_features, width = features.shape
    batch = out.shape[0]
    hidden = width - 2 * batch
    halves = hidden // P
    quarters = 4
    quarter = batch // quarters
    units = P // quarters
    assert quarter == P and batch == 512 and halves == 2

    TC = TILES_PER_CHUNK
    chunks = n_features // (P * TC)
    looped = chunks - FIRST_LOOPED - LAST_CHUNKS
    assert n_features == chunks * P * TC and looped % SLOTS == 0
    turns = looped // SLOTS

    W = slice(0, hidden)
    WHITE = slice(hidden, hidden + batch)
    BLACK = slice(hidden + batch, width)
    ALL = slice(0, width)
    SIDES = (WHITE, BLACK)
    WHITE_0 = slice(hidden, hidden + batch // 2)
    WHITE_1 = slice(hidden + batch // 2, hidden + batch)
    W_WHITE = slice(0, BLACK.start)
    FIRST_PARTS = (slice(0, WHITE_0.stop), WHITE_1, BLACK)
    HALVES = (W_WHITE, BLACK)
    WHITE_BLOCKS, BLACK_BLOCKS = (0, 1), (2, 3)

    CLIP_PIECES = ((0, 2), (2, 4))

    n_h1 = 2 * halves * units
    H2_AT, OUT_AT, B_IN_AT = n_h1, n_h1 + P, n_h1 + P + quarters
    n_params = B_IN_AT + halves
    assert params.shape[1] == n_params

    chunk_dram = features.rearrange("(c p t) n -> c p t n", p=P, t=TC)
    out_dram = out.rearrange("(j n) o -> j (n o)", j=quarters)

    with ExitStack() as ctx:
        def sb(name, shape, dt):
            return ctx.enter_context(nc.sbuf_tensor(name, shape, dt))

        def psum(name, shape):
            return ctx.enter_context(nc.psum_tensor(name, shape, F32))

        def sem(name):
            return ctx.enter_context(nc.semaphore(name))

        raw = [sb(f"raw{s}", [P, TC, width], F32) for s in range(SLOTS)]
        hi = [sb(f"hi{s}", [P, TC, width], F32R) for s in range(SLOTS)]
        lo = [sb(f"lo{s}", [P, TC, width], F32R) for s in range(SLOTS)]
        par = sb("par", [P, n_params], F32)
        rows = sb("rows", [1, bias_rows.shape[1]], F32)
        ones_row = nc.const_aps.tensor(1.0, [1, P], F32)
        ones_block = nc.const_aps.tensor(1.0, [P, P], BF16)
        x_relu = sb("x_relu", [P, 4, batch], F32)
        x_act = sb("x_act", [P, 4, batch], F32)
        h1_act = sb("h1_act", [P, P], F32)
        h2_act = sb("h2_act", [P, P], F32)
        y = sb("y", [quarters, P], F32)

        x_acc = [psum(f"x_acc{b}", [P, batch]) for b in range(4)]
        h1_acc = psum("h1_acc", [P, 512])
        h2_acc = psum("h2_acc", [P, 512])
        y_acc = psum("y_acc", [P, 512])
        warm = psum("warm", [P, 512])

        slot_loaded = [sem(f"slot_loaded{s}") for s in range(SLOTS)]
        first_loaded = [sem(f"first_loaded{i}") for i in range(len(FIRST_PARTS))]
        early_loaded = [[sem(f"early_loaded{n}_{h}") for h in range(2)] for n in range(1, EARLY * TC)]
        tile_loaded = [sem(f"tile_loaded{n}") for n in range(EARLY * TC, SLOTS * TC)]
        params_loaded = sem("params_loaded")
        rows_loaded = sem("rows_loaded")
        first_hi = sem("first_hi")
        first_w_hi = sem("first_w_hi")
        first_lo = sem("first_lo")
        hi_ready = sem("hi_ready")
        lo_ready = sem("lo_ready")
        chunks_used = sem("chunks_used")
        x_summed = sem("x_summed")
        x_relu_ready = sem("x_relu_ready")
        x_ready = sem("x_ready")
        h1_summed = sem("h1_summed")
        h1_ready = sem("h1_ready")
        h2_summed = sem("h2_summed")
        h2_ready = sem("h2_ready")
        y_summed = sem("y_summed")
        y_ready = sem("y_ready")
        y_stored = sem("y_stored")

        block = ctx.enter_context(nc.Block())


        @block.sync
        def _(sp):
            for cols, loaded in zip(FIRST_PARTS, first_loaded):
                sp.dma_start(raw[0][:, 0, cols], chunk_dram[0, :, 0, cols]).then_inc(loaded, 16)
            for n in range(1, EARLY * TC):
                c, t = divmod(n, TC)
                for cols, loaded in zip(HALVES, early_loaded[n - 1]):
                    sp.dma_start(raw[c][:, t, cols], chunk_dram[c, :, t, cols]).then_inc(loaded, 16)
            for n in range(EARLY * TC, SLOTS * TC):
                c, t = divmod(n, TC)
                sp.dma_start(raw[c][:, t, :], chunk_dram[c, :, t, :]).then_inc(tile_loaded[n - EARLY * TC], 16)
            sp.dma_start(rows[:, :], bias_rows).then_inc(rows_loaded, 16)
            sp.dma_start(par[:, :], params).then_inc(params_loaded, 16)
            with sp.Fori(0, turns) as turn:
                for i in range(SLOTS):
                    sp.wait_ge(lo_ready, turn * (2 * SLOTS * TC) + 2 * ((i + 1) * TC - 1))
                    sp.dma_start(raw[i][:, :, :], chunk_dram[turn * SLOTS + (SLOTS + i)]).then_inc(slot_loaded[i], 16)
            sp.wait_ge(y_ready, 1)
            sp.dma_start(out_dram, y[:, :]).then_inc(y_stored, 16)
            sp.wait_ge(y_stored, 16)

        @block.scalar
        def _(act):
            def high_part(s, t, cols, signal, n=1):
                act.activation(hi[s][:, t, cols], raw[s][:, t, cols], ACT.Copy).then_inc(signal, n)

            for part, cols in enumerate((WHITE_0, WHITE_1, BLACK)):
                act.wait_ge(first_loaded[part], 16)
                high_part(0, 0, cols, first_hi)
            for n in range(1, EARLY * TC):
                for cols, loaded in zip(HALVES, early_loaded[n - 1]):
                    act.wait_ge(loaded, 16)
                    high_part(n // TC, n % TC, cols, hi_ready)
            for n in range(EARLY * TC, SLOTS * TC):
                act.wait_ge(tile_loaded[n - EARLY * TC], 16)
                high_part(n // TC, n % TC, ALL, hi_ready, 2)

            with act.Fori(0, turns) as turn:
                for i in range(SLOTS):
                    act.wait_ge(slot_loaded[i], turn * 16 + 16)
                    act.wait_ge(chunks_used, turn * SLOTS + (i + 1))
                    for t in range(TC):
                        high_part(i, t, ALL, hi_ready, 2)

            act.wait_ge(params_loaded, 16)
            for b in range(4):
                act.wait_ge(x_summed, b + 1)
                for first, end in CLIP_PIECES:
                    cols = slice(first * quarter, end * quarter)
                    act.activation(x_relu[:, b, cols], x_acc[b][:, cols], ACT.Relu,
                                   bias=par[:, B_IN_AT + b % 2:B_IN_AT + b % 2 + 1]).then_inc(x_relu_ready, 1)

        @block.vector
        def _(dve):
            def low_part(s, t, cols, signal, n=1):
                dve.tensor_tensor(lo[s][:, t, cols], raw[s][:, t, cols], hi[s][:, t, cols].bitcast(F32),
                                  ALU.subtract).then_inc(signal, n)

            dve.wait_ge(first_loaded[0], 16)
            dve.tensor_copy(hi[0][:, 0, W], raw[0][:, 0, W]).then_inc(first_w_hi, 1)
            dve.wait_ge(first_w_hi, 1)
            low_part(0, 0, W, first_lo)
            dve.wait_ge(first_hi, 2)
            low_part(0, 0, WHITE, first_lo)
            dve.wait_ge(first_hi, 3)
            low_part(0, 0, BLACK, first_lo)
            for n in range(1, EARLY * TC):
                for h, cols in enumerate(HALVES):
                    dve.wait_ge(hi_ready, 2 * n - 1 + h)
                    low_part(n // TC, n % TC, cols, lo_ready)
            for n in range(EARLY * TC, SLOTS * TC):
                dve.wait_ge(hi_ready, 2 * n)
                low_part(n // TC, n % TC, ALL, lo_ready, 2)

            with dve.Fori(0, turns) as turn:
                for i in range(SLOTS):
                    dve.wait_ge(chunks_used, turn * SLOTS + (i + 1))
                    for t in range(TC):
                        dve.wait_ge(hi_ready, turn * (2 * SLOTS * TC) + 2 * ((SLOTS + i) * TC + t))
                        low_part(i, t, ALL, lo_ready, 2)

            for b in range(4):
                for piece, (first, end) in enumerate(CLIP_PIECES):
                    cols = slice(first * quarter, end * quarter)
                    dve.wait_ge(x_relu_ready, len(CLIP_PIECES) * b + piece + 1)
                    dve.tensor_scalar(x_act[:, b, cols], x_relu[:, b, cols], 1.0, None, ALU.min).then_inc(x_ready, 1)
            dve.wait_ge(h1_summed, 1)
            dve.tensor_scalar(h1_act[:, :], h1_acc[:, 0:P], 0.0, 1.0, ALU.max, ALU.min).then_inc(h1_ready, 1)
            dve.wait_ge(h2_summed, 1)
            dve.tensor_scalar(h2_act[:, :], h2_acc[:, 0:P], 0.0, 1.0, ALU.max, ALU.min).then_inc(h2_ready, 1)
            dve.wait_ge(y_summed, 1)
            dve.tensor_copy(y[:, :], y_acc[0:quarters, 0:P]).then_inc(y_ready, 1)

        @block.tensor
        def _(pe):
            def product(b, w_part, x_part, s, t, cols=slice(0, batch), start=False, stop=False):
                side, half = divmod(b, halves)
                x_cols = slice(SIDES[side].start + cols.start, SIDES[side].start + cols.stop)
                return pe.matmul(x_acc[b][:, cols], w_part[s][:, t, half * P:(half + 1) * P],
                                 x_part[s][:, t, x_cols], start=start, stop=stop)

            def tile(n, s, t, by_halves):
                pe.wait_ge(hi_ready, n * 2 - (1 if by_halves else 0))
                for b in WHITE_BLOCKS:
                    product(b, hi, hi, s, t)
                if by_halves:
                    pe.wait_ge(hi_ready, n * 2)
                for b in BLACK_BLOCKS:
                    product(b, hi, hi, s, t)
                pe.wait_ge(lo_ready, n * 2 - (1 if by_halves else 0))
                for b in WHITE_BLOCKS:
                    product(b, hi, lo, s, t)
                for b in WHITE_BLOCKS + BLACK_BLOCKS:
                    product(b, lo, hi, s, t)
                if by_halves:
                    pe.wait_ge(lo_ready, n * 2)
                for b in BLACK_BLOCKS:
                    last = product(b, hi, lo, s, t)
                return last

            for _ in range(WARM_UP_MATMULS):
                pe.matmul(warm[:, 0:P], ones_block, ones_block, start=True, stop=True)

            pe.wait_ge(first_w_hi, 1)
            for q in range(2):
                pe.wait_ge(first_hi, q + 1)
                for b in WHITE_BLOCKS:
                    product(b, hi, hi, 0, 0, slice(q * batch // 2, (q + 1) * batch // 2), start=(q == 0))
            pe.wait_ge(first_lo, 1)
            for b in WHITE_BLOCKS:
                product(b, lo, hi, 0, 0)
            pe.wait_ge(first_lo, 2)
            for b in WHITE_BLOCKS:
                product(b, hi, lo, 0, 0)
            pe.wait_ge(first_hi, 3)
            for b in BLACK_BLOCKS:
                product(b, hi, hi, 0, 0, start=True)
                product(b, lo, hi, 0, 0)
            pe.wait_ge(first_lo, 3)
            for b in BLACK_BLOCKS:
                product(b, hi, lo, 0, 0)
            for n in range(1, FIRST_LOOPED * TC):
                s, t = divmod(n, TC)
                last = tile(n, s, t, by_halves=True)
                if t == TC - 1:
                    last.then_inc(chunks_used, 1)

            with pe.Fori(0, turns) as turn:
                for i in range(SLOTS):
                    for t in range(TC):
                        n = turn * (SLOTS * TC) + ((FIRST_LOOPED + i) * TC + t)
                        last = tile(n, (FIRST_LOOPED + i) % SLOTS, t, by_halves=False)
                    last.then_inc(chunks_used, 1)

            def h1_products(b):
                for piece, (first, end) in enumerate(CLIP_PIECES):
                    pe.wait_ge(x_ready, len(CLIP_PIECES) * b + piece + 1)
                    for j in range(first, end):
                        last = pe.matmul(h1_acc[j * units:(j + 1) * units, 0:P], par[:, b * units:(b + 1) * units],
                                         x_act[:, b, j * quarter:(j + 1) * quarter],
                                         start=False, stop=(b == 3), skip_group_check=True)
                return last

            pe.wait_ge(hi_ready, 2 * (chunks * TC - 1))
            pe.wait_ge(lo_ready, 2 * (chunks * TC - 1))
            for b in range(4):
                if b == 1:
                    pe.wait_ge(rows_loaded, 16)
                    pe.wait_ge(params_loaded, 16)
                    pe.matmul(h1_acc[:, 0:P], rows[:, 0:P], ones_row, start=True, stop=False, skip_group_check=True)
                    pe.matmul(h2_acc[:, 0:P], rows[:, P:2 * P], ones_row, start=True, stop=False)
                    pe.matmul(y_acc[0:quarters, 0:P], rows[:, 2 * P:2 * P + quarters], ones_row, start=True, stop=False)
                tiles = [((chunks - LAST_CHUNKS) * TC + n) for n in range(LAST_CHUNKS * TC)]
                for n in tiles:
                    for w_part, x_part in ((hi, hi), (hi, lo), (lo, hi)):
                        last = product(b, w_part, x_part, n // TC % SLOTS, n % TC,
                                       stop=(n == tiles[-1] and w_part is lo))
                last.then_inc(x_summed, 1)
                if b >= 1:
                    h1_products(b - 1)
            h1_products(3).then_inc(h1_summed, 1)
            pe.wait_ge(h1_ready, 1)
            pe.matmul(h2_acc[:, 0:P], par[:, H2_AT:H2_AT + P], h1_act[:, :], start=False, stop=True).then_inc(h2_summed, 1)
            pe.wait_ge(h2_ready, 1)
            pe.matmul(y_acc[0:quarters, 0:P], par[:, OUT_AT:OUT_AT + quarters], h2_act[:, :],
                      start=False, stop=True).then_inc(y_summed, 1)


def kernel(r_white_features, r_black_features, L0_rec_w_in, L0_rec_b_in, L0_rec_w_h1, L0_rec_b_h1,
           L0_rec_w_h2, L0_rec_b_h2, L0_rec_w_out, L0_rec_b_out):
    import numpy as np
    import concourse.bacc as bacc
    from concourse.bass_utils import run_bass_kernel_spmd

    white, black, w_in = (np.asarray(a) for a in (r_white_features, r_black_features, L0_rec_w_in))
    w_h1, w_h2, w_out = (np.asarray(a) for a in (L0_rec_w_h1, L0_rec_w_h2, L0_rec_w_out))
    b_in, b_h1, b_h2, b_out = (np.asarray(a) for a in (L0_rec_b_in, L0_rec_b_h1, L0_rec_b_h2, L0_rec_b_out))
    batch = white.shape[0]
    units, joined = w_h1.shape
    quarters = P // units

    features = np.ascontiguousarray(np.concatenate([w_in.T, white.T, black.T], axis=1))

    h1_part = w_h1.T.reshape(joined // P, P, units).transpose(1, 0, 2).reshape(P, -1)
    h2_part = np.zeros((P, P), w_h2.dtype)
    out_part = np.zeros((P, quarters), w_out.dtype)
    for j in range(quarters):
        h2_part[j * units:(j + 1) * units, j * units:(j + 1) * units] = w_h2.T
        out_part[j * units:(j + 1) * units, j] = w_out[0]
    params = np.ascontiguousarray(np.concatenate([h1_part, h2_part, out_part, b_in.reshape(-1, P).T], axis=1))
    bias_rows = np.concatenate([np.tile(b_h1, quarters), np.tile(b_h2, quarters), np.tile(b_out, quarters)])[None]

    nc = bacc.Bacc("TRN2", target_bir_lowering=False, num_devices=1)
    arrays = {"features": features, "params": params, "bias_rows": bias_rows}
    ins = [nc.dram_tensor(n, a.shape, mybir.dt.from_np(a.dtype), kind="ExternalInput").ap() for n, a in arrays.items()]
    out = nc.dram_tensor("out", (batch, 1), F32, kind="ExternalOutput").ap()
    build(nc, *ins, out)
    result = run_bass_kernel_spmd(nc, [arrays], core_ids=[0])
    return result.results[0]["out"]
```
